# Optimizing a Trainium2 kernel written in Bass

```python
import numpy as np
import jax
import jax.numpy as jnp

def _softmax(x, axis=-1):
    return jax.nn.softmax(x, axis=axis)
def _gelu(x):
    return jax.nn.gelu(x, approximate=True)
def _silu(x):
    return jax.nn.silu(x)
def _sigmoid(x):
    return jax.nn.sigmoid(x)
def _layernorm(x, axis=-1, eps=1e-5):
    m = jnp.mean(x, axis=axis, keepdims=True)
    v = jnp.var(x, axis=axis, keepdims=True)
    return (x - m) / jnp.sqrt(v + eps)
def _scatter_add(tgt, idx, src, axis=0):
    return tgt.at[idx].add(src)
def _segment_sum(src, seg, n):
    return jax.ops.segment_sum(src, seg, n)

kernel_name = 'mk_adj_preln_d2_adj_64_ec429f'

def setup_inputs(seed: int = 0):
    np.random.seed(seed)
    _w = jnp.asarray
    def _rec_inputs():
        import jax
        import jax.numpy as jnp
        _gk = jax.random.key(seed)
        x = -0.001547 + 1.001 * jax.random.normal(jax.random.fold_in(_gk, 1), (8192, 64), jnp.float32)
        _a = jax.random.bernoulli(jax.random.fold_in(_gk, 2), 0.000976562, (8192, 8192))
        _a = jnp.logical_or(_a, jnp.swapaxes(_a, -1, -2))
        _a = jnp.logical_or(_a, jnp.eye(8192, dtype=bool))
        adj = _a.astype(jnp.int32)
        return x, adj
    x, adj = _rec_inputs()
    def _L0_gnn_setup():
        import jax, jax.numpy as jnp
        import numpy as np
        N = 4096
        C = 64
        GDEP = 2
        HID = 32
        ALPHA = 0.2
        NEG_INF = jnp.float32(-9000000000000000.0)

        def _gat_layer(h, adj_mask, W_l, lw, lb, a):
            Wh = h @ W_l
            L1, L2 = (lw[:C], lw[C:])
            u = Wh @ L1 @ a
            v = Wh @ L2 @ a
            c = lb @ a
            e = jax.nn.leaky_relu(u + v.T + c, negative_slope=ALPHA)
            scores = jnp.where(adj_mask, e, NEG_INF)
            att = jax.nn.softmax(scores, axis=1)
            return jax.nn.elu(att @ Wh)
        key = jax.random.key(seed)
        ks = jax.random.split(key, 8)
        x = jax.random.normal(ks[0], (N, C), jnp.float32)
        adj = jax.random.randint(ks[1], (N, N), 0, 2, jnp.int32)
        W = jax.random.normal(ks[2], (GDEP, C, C), jnp.float32) / np.sqrt(C)
        lin_w = jax.random.normal(ks[3], (GDEP, 2 * C, HID), jnp.float32) / np.sqrt(2 * C)
        lin_b = jnp.zeros((GDEP, HID), jnp.float32)
        attn = jax.random.normal(ks[4], (GDEP, HID, 1), jnp.float32) / np.sqrt(HID)
        mlp_w = jax.random.normal(ks[5], ((GDEP + 1) * C, C), jnp.float32) / np.sqrt((GDEP + 1) * C)
        mlp_b = jnp.zeros((C,), jnp.float32)
        return dict(x=x, adj=adj, W=W, lin_w=lin_w, lin_b=lin_b, attn=attn, mlp_w=mlp_w, mlp_b=mlp_b)
    _L0_gnn_all = _L0_gnn_setup()
    _L0_gnn_in = {k: v for k, v in _L0_gnn_all.items() if k in ('W', 'lin_w', 'lin_b', 'attn', 'mlp_w', 'mlp_b', )}
    del _L0_gnn_all

    def _L1_gnn_setup():
        import jax, jax.numpy as jnp
        import numpy as np
        N = 20000
        F = 64
        O = 64
        key = jax.random.key(seed)
        k1, k2, k3 = jax.random.split(key, 3)
        x = jax.random.normal(k1, (N, F), dtype=jnp.float32)
        adj = jax.random.randint(k2, (N, N), 0, 2, dtype=jnp.int32)
        stdv = float(np.sqrt(6.0 / (2 * F + O)))
        weight = jax.random.uniform(k3, (2 * F, O), dtype=jnp.float32, minval=-stdv, maxval=stdv)
        bias = jnp.zeros((O,), dtype=jnp.float32)
        return {'x': x, 'adj': adj, 'weight': weight, 'bias': bias}
    _L1_gnn_all = _L1_gnn_setup()
    _L1_gnn_in = {k: v for k, v in _L1_gnn_all.items() if k in ('weight', 'bias', )}
    del _L1_gnn_all

    return {
        "x": x,
        "adj": adj,
        "L0_gnn_W": _L0_gnn_in["W"],
        "L0_gnn_lin_w": _L0_gnn_in["lin_w"],
        "L0_gnn_lin_b": _L0_gnn_in["lin_b"],
        "L0_gnn_attn": _L0_gnn_in["attn"],
        "L0_gnn_mlp_w": _L0_gnn_in["mlp_w"],
        "L0_gnn_mlp_b": _L0_gnn_in["mlp_b"],
        "L1_gnn_weight": _L1_gnn_in["weight"],
        "L1_gnn_bias": _L1_gnn_in["bias"],
    }

def reference(x, adj, L0_gnn_W, L0_gnn_lin_w, L0_gnn_lin_b, L0_gnn_attn, L0_gnn_mlp_w, L0_gnn_mlp_b, L1_gnn_weight, L1_gnn_bias):
    import jax
    import jax.numpy as jnp
    def _L0_gnn_ref(x, adj, W, lin_w, lin_b, attn, mlp_w, mlp_b):
        import jax, jax.numpy as jnp
        import numpy as np
        N = 4096
        C = 64
        GDEP = 2
        HID = 32
        ALPHA = 0.2
        NEG_INF = jnp.float32(-9000000000000000.0)

        def _gat_layer(h, adj_mask, W_l, lw, lb, a):
            Wh = h @ W_l
            L1, L2 = (lw[:C], lw[C:])
            u = Wh @ L1 @ a
            v = Wh @ L2 @ a
            c = lb @ a
            e = jax.nn.leaky_relu(u + v.T + c, negative_slope=ALPHA)
            scores = jnp.where(adj_mask, e, NEG_INF)
            att = jax.nn.softmax(scores, axis=1)
            return jax.nn.elu(att @ Wh)
        mask = adj > 0
        h = x
        outs = [h]
        for i in range(GDEP):
            h = ALPHA * x + (1.0 - ALPHA) * _gat_layer(h, mask, W[i], lin_w[i], lin_b[i], attn[i])
            outs.append(h)
        ho = jnp.concatenate(outs, axis=-1)
        return ho @ mlp_w + mlp_b

    def _L1_gnn_ref(x, adj, weight, bias):
        import jax, jax.numpy as jnp
        import numpy as np
        N = 20000
        F = 64
        O = 64
        a = (adj == 1).astype(x.dtype)
        deg = jnp.sum(a, axis=1, keepdims=True)
        x1 = a @ x / deg
        n_x = jnp.concatenate([x1, x], axis=1)
        return n_x @ weight + bias

    h = jnp.maximum(_layernorm(x, axis=-1), 0.0)
    x = x + _L0_gnn_ref(h, adj, L0_gnn_W, L0_gnn_lin_w, L0_gnn_lin_b, L0_gnn_attn, L0_gnn_mlp_w, L0_gnn_mlp_b)
    h = jnp.maximum(_layernorm(x, axis=-1), 0.0)
    x = x + _L1_gnn_ref(h, adj, L1_gnn_weight, L1_gnn_bias)
    return x


_drawn_inputs = setup_inputs


def setup_inputs(seed=0):
    import zlib

    import numpy as np

    out = dict(_drawn_inputs(seed))
    spreads = {'L0_gnn_lin_b': (0.0, 0.8), 'L0_gnn_mlp_b': (0.0, 0.1), 'L1_gnn_bias': (0.0, 0.1)}
    factors = {'L0_gnn_lin_w': 3.44, 'L0_gnn_attn': 3.469}
    for name, (base, spread) in spreads.items():
        noise = np.random.default_rng([zlib.crc32(name.encode()), seed]).standard_normal(out[name].shape)
        drawn = base * np.exp(spread * noise) if base else spread * noise
        out[name] = jnp.asarray(drawn.astype(out[name].dtype))
    for name, factor in factors.items():
        out[name] = (out[name] * factor).astype(out[name].dtype)
    return out
```

```python
import concourse.bass as bass
from concourse import mybir
from contextlib import ExitStack

FP32 = mybir.dt.float32
BF16 = mybir.dt.bfloat16
FP16 = mybir.dt.float16
FP8 = mybir.dt.float8e4
I32 = mybir.dt.int32
U32 = mybir.dt.uint32
U8 = mybir.dt.uint8
I8 = mybir.dt.int8
ALU = mybir.AluOpType
ACT = mybir.ActivationFunctionType
AX = mybir.AxisListType
RMAX = bass.bass_isa.ReduceOp.max

P = 128
N = 8192
C = 64
CE = C + 1
HID = 32
T = N // P
ALPHA = 0.2
EPS = 1e-5
SHIFT = 60.0
CHJ = 1024
NCH = N // CHJ
QC = CHJ // 256
TC = CHJ // P
RG1 = 512
IT1 = RG1 // P
NG1 = N // RG1
RG2 = 1024
IT2 = RG2 // P
NG2 = N // RG2
CB = CHJ * RG1 // P
WC = 3 * CE
ONE = 0x38383838
FSC = 4096.0


class Chain:

    def __init__(self, eng, sem, base=0):
        self.eng, self.sem, self.base, self.k = eng, sem, base, 0

    def step(self, ins):
        self.k += 1
        ins.then_inc(self.sem, 1)
        wait_apart(self.eng, self.sem, self.base + self.k)


def wait_apart(eng, sem, value):
    eng.wait_ge(sem, value)
    eng.nop(nofuse=True)


def prime(eng, *sems, by=1):
    for sem in sems:
        eng.sem_inc(sem, by)


def wait_primed(eng, sem, value):
    wait_apart(eng, sem, value + 1)


def gnn_program(nc, x, adj, w, lin_w, lin_b, attn, mlp_w, mlp_b, w1, bias1, out):
    ctx = ExitStack()
    with ctx:
        def sb(name, shape, dt):
            return ctx.enter_context(nc.sbuf_tensor(name, shape, dt))

        def sem(name):
            return ctx.enter_context(nc.semaphore(name))

        codes_d = nc.dram_tensor("codes_d", (NG1, NCH, P, CB), U8).ap()
        h0_d = nc.dram_tensor("h0_d", (P, T * C), FP32).ap()
        xres_d = nc.dram_tensor("xres_d", (P, T * C), FP32).ap()

        urow = sb("urow", [P, N], FP32)
        wsplit = sb("wsplit", [P, T, 2 * WC], BF16)
        hw = sb("hw", [P, T, CE], FP32)
        vu = sb("vu", [P, T, 2], FP32)
        negv = sb("negv", [P, T], FP32)
        rowf = sb("rowf", [P, T, 2], FP32)
        expv = sb("expv", [P, T, 2], FP32)
        meanw = sb("meanw", [P, CE], FP32)
        sm = sb("sm", [P, 8 * T], FP32)
        rsum = sb("rsum", [P, IT2, 2, CE], FP32)
        pa = sb("pa", [P, IT2, CE], FP32)
        pb = sb("pb", [P, IT2, CE], FP32)
        nonb = sb("nonb", [P, IT2], FP32)
        identf = sb("identf", [P, P], FP32)
        identb = sb("identb", [P, P], BF16)
        zeros = sb("zeros", [P, 512], BF16)
        onesf = sb("onesf", [P, P], FP32)
        waug = sb("waug", [C, 3, C + 2 + C], FP32)
        wub = sb("wub", [C, 2, P], FP32)
        wt = sb("wt", [C, 2, C], FP32)
        lwt = sb("lwt", [HID, 2, 2 * C], FP32)
        att = sb("att", [HID, 2], FP32)
        lb = sb("lb", [HID, 2], FP32)
        lbb = sb("lbb", [HID, 2, P], FP32)
        la = sb("la", [C, 2, 2], FP32)
        cb = sb("cb", [P, 2], FP32)
        w1s = sb("w1s", [2 * C, C], FP32)
        mlpb = sb("mlpb", [P, C], FP32)
        b1b = sb("b1b", [P, C], FP32)
        region = sb("region", [P, 80 * 1024], U8)

        def at(off, n, dt):
            return region[:, off:off + n].bitcast(dt)

        KB = 1024
        bank = [ctx.enter_context(nc.psum_tensor(f"bank{i}", [P, 512], FP32)) for i in range(8)]

        ht = at(0, 32 * KB, FP32)[0:C, :]
        xr = at(32 * KB, 16 * KB, FP32).rearrange("p (t c) -> p t c", c=C)
        h0 = at(48 * KB, 16 * KB, FP32).rearrange("p (t c) -> p t c", c=C)
        tmp = at(64 * KB, 16 * KB, FP32)
        cen = at(0, 16 * KB, FP32).rearrange("p (t c) -> p t c", c=C)
        sqr = at(16 * KB, 16 * KB, FP32).rearrange("p (t c) -> p t c", c=C)
        nx = at(48 * KB, 32 * KB, FP32).rearrange("p (t c) -> p t c", c=2 * C)
        wf16 = wsplit[:, :, :].rearrange("p t c -> p (t c)")[:, 0:T * (2 * C + 1)].bitcast(FP16) \
            .rearrange("p (t c) -> p t c", c=2 * C + 1)
        x_v = x.rearrange("(q p b) c -> p q (b c)", p=P, b=2)
        out_v = out.rearrange("(q p b) c -> p q (b c)", p=P, b=2)

        def pairs(ap):
            return ap.rearrange("p (q b) c -> p q (b c)", b=2)

        def layer_norm(dve, act, name, dst):
            s_c, s_cen, s_sq, s_rv, s_sd, s_h = (sem(f"{name}_{x}") for x in
                                                 ("chain", "centred", "squares", "recip", "root", "done"))
            mean, var = sm[:, 0:T], sm[:, T:2 * T]
            rec, root = sm[:, 2 * T:3 * T], sm[:, 3 * T:4 * T]

            def bc(v):
                return v.unsqueeze(2).to_broadcast([P, T, C])

            def on_vector(dve):
                ch = Chain(dve, s_c)
                ch.step(nc.vector.tensor_reduce(mean, xr, AX.X, ALU.add))
                ch.step(nc.vector.tensor_scalar(mean, mean, 1.0 / C, None, ALU.mult))
                nc.vector.tensor_tensor(cen, xr, bc(mean), ALU.subtract).then_inc(s_cen, 1)
                dve.wait_ge(s_sq, 1)
                ch.step(nc.vector.tensor_reduce(var, sqr, AX.X, ALU.add))
                ch.step(nc.vector.tensor_scalar(var, var, 1.0 / C, EPS, ALU.mult, ALU.add))
                nc.vector.reciprocal(rec, var).then_inc(s_rv, 1)
                dve.wait_ge(s_sd, 1)
                ch.step(nc.vector.tensor_tensor(cen, cen, bc(root), ALU.mult))
                nc.vector.tensor_scalar(dst, cen, 0.0, None, ALU.max).then_inc(s_h, 1)

            def on_scalar(act):
                act.wait_ge(s_cen, 1)
                nc.scalar.activation(sqr, cen, ACT.Square).then_inc(s_sq, 1)
                act.wait_ge(s_rv, 1)
                nc.scalar.activation(root, rec, ACT.Sqrt).then_inc(s_sd, 1)

            return on_vector, on_scalar, s_h

        x_in = sem("x_loaded")
        wts = sem("weights_loaded")
        const = sem("constants_made")
        la_p, la_s, wa_p, wa_s = sem("lin_attn_product"), sem("lin_attn_copied"), sem("w_attn_product"), sem("w_attn_copied")
        lbs, h0_st, prep = sem("bias_spread"), sem("h0_stored"), sem("x_bias_chain")
        ln0_v, ln0_s, ln0_done = layer_norm(None, None, "ln0", hw[:, :, 0:C])
        NW = 16
        with nc.Block() as block:
            @block.sync
            def _(sp):
                sp.dma_start(pairs(xr), x_v).then_inc(x_in, 16)
                sp.dma_start(waug[:, 0:2, 0:C], w.rearrange("l c o -> c l o")).then_inc(wts, 16)
                sp.dma_start(waug[:, :, C + 2:], mlp_w.rearrange("(l c) o -> c l o", c=C)).then_inc(wts, 16)
                sp.dma_start(w1s[:, :], w1).then_inc(wts, 16)
                for l in range(2):
                    sp.dma_start(wt[:, l, :], w[l].rearrange("c o -> o c"), allow_slow_non_contiguous=True).then_inc(wts, 16)
                    sp.dma_start(lwt[:, l, :], lin_w[l].rearrange("c h -> h c"), allow_slow_non_contiguous=True).then_inc(wts, 16)
                sp.dma_start(att[:, :], attn.rearrange("l h o -> h (l o)"), allow_slow_non_contiguous=True).then_inc(wts, 16)
                sp.dma_start(lb[:, :], lin_b.rearrange("l h -> h l"), allow_slow_non_contiguous=True).then_inc(wts, 16)
                sp.dma_start(mlpb[:, :], mlp_b.partition_broadcast(P)).then_inc(wts, 16)
                sp.dma_start(b1b[:, :], bias1.partition_broadcast(P)).then_inc(wts, 16)
                sp.wait_ge(ln0_done, 1)
                sp.dma_start(h0_d.rearrange("p (t c) -> p t c", c=C), hw[:, :, 0:C]).then_inc(h0_st, 16)

            NWT = 16 * 11

            @block.gpsimd
            def _(pool):
                nc.gpsimd.memset(identf[:, :], 0.0).then_inc(const, 1)
                nc.gpsimd.memset(zeros[:, :], 0.0).then_inc(const, 1)
                nc.gpsimd.memset(onesf[:, :], 1.0).then_inc(const, 1)
                pool.wait_ge(const, 3)
                nc.gpsimd.affine_select(out=identf[:, :], in_=identf[:, :], compare_op=ALU.not_equal, fill=1.0,
                                        base=0, pattern=[[-1, P]], channel_multiplier=1).then_inc(const, 1)
                pool.wait_ge(const, 4)
                nc.gpsimd.tensor_copy(identb[:, :], identf[:, :]).then_inc(const, 1)

            @block.scalar
            def _(act):
                ln0_s(act)

            @block.vector
            def _(dve):
                dve.wait_ge(x_in, 16)
                ln0_v(dve)
                dve.wait_ge(wts, NWT)
                nc.vector.tensor_copy(lbb[:, :, :], lb[:, :].unsqueeze(2).to_broadcast([HID, 2, P])).then_inc(lbs, 1)
                dve.wait_ge(ln0_done, 1)
                nc.vector.tensor_tensor(xr, xr, mlpb[:, :].unsqueeze(1).to_broadcast([P, T, C]), ALU.add).then_inc(prep, 1)
                dve.wait_ge(la_p, 1)
                nc.vector.tensor_copy(la[:, :, :], bank[0][0:C, 0:4].rearrange("p (l k) -> p l k", k=2)).then_inc(la_s, 1)
                dve.wait_ge(wa_p, 1)
                ch = Chain(dve, wa_s)
                ch.step(nc.vector.tensor_copy(waug[:, 0:2, C:C + 2], bank[1][0:C, 0:4].rearrange("p (l k) -> p l k", k=2)))
                ch.step(nc.vector.tensor_copy(cb[:, :], bank[2][:, 0:2]))
                ch.step(nc.vector.tensor_copy(wub[:, :, :], waug[:, 0:2, C + 1:C + 2].to_broadcast([C, 2, P])))

            @block.tensor
            def _(pe):
                pe.wait_ge(wts, NWT)
                for l in range(2):
                    for k in range(2):
                        last = nc.tensor.matmul(bank[0][0:C, 2 * l + k:2 * l + k + 1],
                                                lwt[:, l, C * (1 - k):C * (2 - k)], att[:, l:l + 1], start=True, stop=True)
                last.then_inc(la_p, 1)
                pe.wait_ge(la_s, 1)
                for l in range(2):
                    nc.tensor.matmul(bank[1][0:C, 2 * l:2 * l + 2], wt[:, l, :], la[:, l, :], start=True, stop=True)
                pe.wait_ge(lbs, 1)
                for l in range(2):
                    last = nc.tensor.matmul(bank[2][:, l:l + 1], lbb[:, l, :], att[:, l:l + 1], start=True, stop=True)
                last.then_inc(wa_p, 1)

        def boundary(l):
            s = lambda n: sem(f"b{l}_{n}")
            loaded, negp, expd, h_ready = s("loaded"), s("neg_part"), s("exp_done"), s("h_ready")
            vch, htp, hte = s("vchain"), s("h_transposed"), s("h_copied")
            prod, out_a, out_v2 = s("products"), s("taken_by_scalar"), s("taken_by_vector")
            vm, vall, col, colp, mean_ok = s("v_max_part"), s("v_max"), s("col_sum"), s("col_product"), s("mean_ready")
            ea, eb = s("exp_args"), s("exps")
            stored = s("stored")
            NB = 16
            HB = 8
            gat = l < 2
            if not gat:
                ln_v, ln_s, ln_done = layer_norm(None, None, "ln1", nx[:, :, C:2 * C])
            minp = lambda k: tmp[:, (k % 2) * 512:(k % 2 + 1) * 512].rearrange("p (t c) -> p t c", c=C)
            expo = lambda k: tmp[:, 1024 + (k % 2) * 512:1024 + (k % 2 + 1) * 512].rearrange("p (t c) -> p t c", c=C)
            vmax, vmall = sm[:, 6 * T:6 * T + 1], sm[:, 6 * T + 1:6 * T + 2]
            cv = sm[:, 6 * T + 2:6 * T + 3]
            rden = sm[:, 5 * T:6 * T]

            ht_all = at(0, 32 * KB, FP32)

            with nc.Block() as block:
                @block.sync
                def _(sp):
                    if l > 0:
                        sp.wait_ge(h0_st, 16)
                        sp.dma_start(h0, h0_d.rearrange("p (t c) -> p t c", c=C)).then_inc(loaded, 16)
                        sp.dma_start(xr, xres_d.rearrange("p (t c) -> p t c", c=C)).then_inc(loaded, 16)
                    if gat:
                        for k in range(4):
                            ts = slice(16 * k, 16 * k + 16)
                            sp.wait_ge(out_v2, 4 * (k + 1))
                            sp.dma_start(xres_d.rearrange("p (t c) -> p t c", c=C)[:, ts, :], xr[:, ts, :]).then_inc(stored, 16)
                        sp.wait_ge(stored, 64)

                @block.tensor
                def _(pe):
                    def transposes(k):
                        if k >= 2:
                            pe.wait_ge(hte, k - 1)
                        if l > 0:
                            pe.wait_ge(h_ready, k // 2 + 1)
                        for i in range(4):
                            last = nc.tensor.transpose(bank[k % 2][0:C, i * P:(i + 1) * P], hw[:, 4 * k + i, 0:C], identf[:, :])
                        last.then_inc(htp, 1)

                    transposes(0)
                    for k in range(NB):
                        if k + 1 < NB:
                            transposes(k + 1)
                        pe.wait_ge(hte, k + 1)
                        if k >= 2:
                            pe.wait_ge(out_v2, k - 1)
                            if gat:
                                pe.wait_ge(out_a, k - 1)
                        if gat:
                            nc.tensor.matmul(bank[2 + k % 2][:, :], wub[:, l, :], ht[:, 512 * k:512 * (k + 1)], start=True, stop=True)
                        for i in range(4):
                            q, b = (4 * k + i) // 2, i % 2
                            lhs = ht[:, 256 * q:256 * (q + 1)].rearrange("c (p b) -> c b p", b=2)[:, b, :]
                            if gat:
                                nc.tensor.matmul(bank[4 + k % 2][:, i * (C + 2):(i + 1) * (C + 2)], lhs, waug[:, l, 0:C + 2],
                                                 start=True, stop=True)
                            last = nc.tensor.matmul(bank[6 + k % 2][:, i * C:(i + 1) * C], lhs, waug[:, l, C + 2:],
                                                    start=True, stop=True)
                        last.then_inc(prod, 1)
                    if gat:
                        pe.wait_ge(col, 1)
                        nc.tensor.matmul(bank[0][:, 0:CE], onesf[:, :], meanw[:, :], start=True, stop=True).then_inc(colp, 1)

                @block.scalar
                def _(act):
                    def exp_part(k):
                        if l > 0:
                            act.wait_ge(negp, k + 1)
                            nc.scalar.activation(expo(k), minp(k), ACT.Exp).then_inc(expd, 1)
                    exp_part(0)
                    if l == 0:
                        act.wait_ge(h0_st, 16)
                    for k in range(NB):
                        if k % 2 == 0 and k // 2 + 1 < HB:
                            exp_part(k // 2 + 1)
                        if gat:
                            act.wait_ge(prod, k + 1)
                            nc.scalar.activation(urow[:, 512 * k:512 * (k + 1)], bank[2 + k % 2][:, :], ACT.Identity,
                                                 bias=cb[:, l:l + 1])
                            pw = bank[4 + k % 2][:, 0:4 * (C + 2)].rearrange("p (t c) -> p t c", c=C + 2)
                            nc.scalar.activation(hw[:, 4 * k:4 * k + 4, 0:C], pw[:, :, 0:C], ACT.Copy)
                            nc.scalar.activation(vu[:, 4 * k:4 * k + 4, :], pw[:, :, C:C + 2], ACT.Copy).then_inc(out_a, 1)
                    if gat:
                        act.wait_ge(ea, 1)
                        nc.scalar.activation(rowf[:, :, :], rowf[:, :, :], ACT.Exp)
                        nc.scalar.activation(expv[:, :, :], expv[:, :, :], ACT.Exp).then_inc(eb, 1)
                    else:
                        ln_s(act)

                @block.vector
                def _(dve):
                    ch = Chain(dve, vch)

                    def rows_finish_a(k):
                        ts = slice(8 * k, 8 * k + 8)
                        ch.step(nc.vector.reciprocal(rden[:, ts], hw[:, ts, C]))
                        ch.step(nc.vector.tensor_tensor(hw[:, ts, 0:C], hw[:, ts, 0:C],
                                                        rden[:, ts].unsqueeze(2).to_broadcast([P, 8, C]), ALU.mult))
                        nc.vector.tensor_scalar(minp(k), hw[:, ts, 0:C], 0.0, None, ALU.min).then_inc(negp, 1)

                    def rows_finish_b(k):
                        ts = slice(8 * k, 8 * k + 8)
                        dve.wait_ge(expd, k + 1)
                        ch.step(nc.vector.scalar_tensor_tensor(hw[:, ts, 0:C], hw[:, ts, 0:C], 0.0, expo(k), ALU.max, ALU.add))
                        ch.step(nc.vector.tensor_scalar(hw[:, ts, 0:C], hw[:, ts, 0:C], -1.0, 1.0 - ALPHA, ALU.add, ALU.mult))
                        nc.vector.scalar_tensor_tensor(hw[:, ts, 0:C], h0[:, ts, :], ALPHA, hw[:, ts, 0:C],
                                                       ALU.mult, ALU.add).then_inc(h_ready, 1)

                    if l > 0:
                        dve.wait_ge(loaded, 32)
                        rows_finish_a(0)
                        rows_finish_a(1)
                        rows_finish_b(0)

                    def copy_ht(k):
                        dve.wait_ge(htp, k + 1)
                        nc.vector.tensor_copy(
                            ht[:, 512 * k:512 * (k + 1)].rearrange("c (q p b) -> c q b p", q=2, b=2),
                            bank[k % 2][0:C, :].rearrange("c (q b p) -> c q b p", q=2, b=2)).then_inc(hte, 1)

                    copy_ht(0)
                    for k in range(NB):
                        if l > 0 and k % 2 == 0 and k // 2 + 1 < HB:
                            if k // 2 + 2 < HB:
                                rows_finish_a(k // 2 + 2)
                            rows_finish_b(k // 2 + 1)
                        if k + 1 < NB:
                            copy_ht(k + 1)
                        dve.wait_ge(prod, k + 1)
                        nc.vector.tensor_tensor(xr[:, 4 * k:4 * k + 4, :], xr[:, 4 * k:4 * k + 4, :],
                                                bank[6 + k % 2][:, 0:4 * C].rearrange("p (t c) -> p t c", c=C),
                                                ALU.add).then_inc(out_v2, 1)
                    dve.wait_ge(out_v2, NB)
                    if gat:
                        dve.wait_ge(out_a, NB)
                        ch.step(nc.vector.memset(hw[:, :, C:CE], 1.0))
                        nc.vector.tensor_reduce(vmax, vu[:, :, 0], AX.X, ALU.max).then_inc(vm, 1)
                        nc.vector.tensor_scalar(negv[:, :], vu[:, :, 0], -1.0, None, ALU.mult)
                        nc.vector.tensor_reduce(meanw[:, :], hw[:, :, :].rearrange("p t c -> p c t"), AX.X, ALU.add).then_inc(col, 1)
                        zt, z2, mx = sm[:, 0:T], sm[:, T:2 * T], sm[:, 2 * T:3 * T]
                        dve.wait_ge(vall, 1)
                        ch.step(nc.vector.tensor_tensor(cv, vmall, cb[:, l:l + 1], ALU.add))
                        nc.vector.tensor_scalar(expv[:, :, 0], vu[:, :, 0], vmall, SHIFT, ALU.subtract, ALU.add)
                        nc.vector.tensor_scalar(expv[:, :, 1], vu[:, :, 0], vmall, ALPHA, ALU.subtract, ALU.mult)
                        ch.step(nc.vector.tensor_scalar(zt, vu[:, :, 1], cv, None, ALU.add))
                        ch.step(nc.vector.tensor_scalar(z2, zt, ALPHA, None, ALU.mult))
                        ch.step(nc.vector.tensor_tensor(mx, zt, z2, ALU.max))
                        ch.step(nc.vector.scalar_tensor_tensor(rowf[:, :, 0], zt, SHIFT, mx, ALU.subtract, ALU.subtract))
                        nc.vector.tensor_tensor(rowf[:, :, 1], z2, mx, ALU.subtract).then_inc(ea, 1)
                        dve.wait_ge(colp, 1)
                        ch.step(nc.vector.tensor_scalar(meanw[:, :], bank[0][:, 0:CE], 1.0 / N, None, ALU.mult))
                        dve.wait_ge(eb, 1)
                    else:
                        ln_v(dve)
                        dve.wait_ge(ln_done, 1)
                        big = ht_all[:, 0:T * C].rearrange("p (t c) -> p t c", c=C)
                        ch.step(nc.vector.tensor_scalar(big, nx[:, :, C:2 * C], FSC, None, ALU.mult))
                        ch.step(nc.vector.tensor_copy(wf16[:, :, 0:C], big))
                        ch.step(nc.vector.tensor_tensor(wf16[:, :, C:2 * C], big, wf16[:, :, 0:C], ALU.subtract))
                        ch.step(nc.vector.memset(wf16[:, :, 2 * C:2 * C + 1], 1.0))

                @block.gpsimd
                def _(pool):
                    if gat:
                        pool.wait_ge(vm, 1)
                        nc.gpsimd.partition_all_reduce(vmall, vmax, P, RMAX).then_inc(vall, 1)

        SPLIT = 5

        def split(ch, eng, s, c, full, rest):
            ts = slice(TC * c, TC * (c + 1))
            part = [wsplit[:, ts, s * WC + j * CE:s * WC + (j + 1) * CE] for j in range(3)]
            ch.step(eng.tensor_tensor(full, hw[:, ts, :], expv[:, ts, s:s + 1].to_broadcast([P, TC, CE]), ALU.mult))
            ch.step(eng.tensor_copy(part[0], full))
            ch.step(eng.tensor_tensor(rest, full, part[0], ALU.subtract))
            ch.step(eng.tensor_copy(part[1], rest))
            ch.step(eng.tensor_tensor(part[2], rest, part[1], ALU.subtract))

        def split_on(ch, c):
            flat = rsum[:, :, :, :].rearrange("p t s c -> p (t s c)")
            split(ch, nc.vector, 0, c, flat[:, 0:TC * CE].rearrange("p (t c) -> p t c", c=CE),
                  flat[:, TC * CE:2 * TC * CE].rearrange("p (t c) -> p t c", c=CE))

        def split_off(ch, c):
            split(ch, nc.gpsimd, 1, c, pa[:, :, :], pb[:, :, :])

        def rows_join(pool, nc, g, nt, ready, used, psem):
            STEPS = 5
            ch = Chain(pool, psem, g * STEPS)
            hwt = hw[:, bass.ds(g * nt, nt), :]
            f = rowf[:, bass.ds(g * nt, nt), :]
            a, b = pa[:, 0:nt, :], pb[:, 0:nt, :]
            ch.step(nc.gpsimd.tensor_tensor(a, rsum[:, 0:nt, 0, :], f[:, :, 0:1].to_broadcast([P, nt, CE]), ALU.mult))
            ch.step(nc.gpsimd.tensor_tensor(b, rsum[:, 0:nt, 1, :], f[:, :, 1:2].to_broadcast([P, nt, CE]), ALU.mult))
            ch.step(nc.gpsimd.tensor_tensor(a, a, b, ALU.add))
            ch.step(nc.gpsimd.tensor_scalar(nonb[:, 0:nt], a[:, :, C], 0.0, None, ALU.is_equal))
            ch.step(nc.gpsimd.tensor_tensor(b, meanw[:, :].unsqueeze(1).to_broadcast([P, nt, CE]),
                                            nonb[:, 0:nt].unsqueeze(2).to_broadcast([P, nt, CE]), ALU.mult))
            nc.gpsimd.tensor_tensor(hwt, a, b, ALU.add).then_inc(used, 1)

        def masks(dve, m8, s8, on, off, on_ready, off_ready, base):
            nc.vector.scalar_tensor_tensor(on, s8, ONE, m8, ALU.bitwise_and, ALU.bitwise_and).then_inc(on_ready, 1)
            wait_primed(dve, on_ready, base + 1)
            nc.vector.scalar_tensor_tensor(off, m8, ONE, on, ALU.bitwise_and, ALU.bitwise_xor).then_inc(off_ready, 1)

        def columns(buf, n_gh, it):
            v = buf.bitcast(FP8).rearrange("k (g q i b) -> k g q b i", g=n_gh, q=QC, b=2)
            gh, r = it // IT1, it % IT1
            q, b = r // 2, r % 2
            return [v[:, gh, t // 2, t % 2, 256 * q:256 * (q + 1)].rearrange("k (p b) -> k b p", b=2)[:, b, :]
                    for t in range(TC)]

        def first_layer():
            s = lambda n: sem(f"f_{n}")
            two = lambda n: [sem(f"f_{n}{i}") for i in range(2)]
            adj_in, coded, tp_done = two("adj_loaded"), two("coded"), two("codes_transposed")
            sgn, on_r, off_r, used = s("signs"), two("on_ready"), two("off_ready"), two("masks_used")
            out_of = [s(f"copied_bank{i}") for i in range(4)]
            m_st = [s(f"codes_stored{i}") for i in range(4)]
            acc_out, joined, pch = s("sums_taken"), s("rows_joined"), s("pool_chain")
            w_on, w_off = s("on_side_split"), s("off_side_split")
            adjb = [at(i * 16 * KB, 16 * KB, I32).rearrange("p (t j) -> p t j", t=IT1) for i in range(2)]
            code = [at(32 * KB + i * 4 * KB, 4 * KB, FP8) for i in range(2)]
            mbuf = [at(40 * KB + i * 4 * KB, 4 * KB, U8) for i in range(4)]
            sbuf_ = [at(56 * KB + i * 4 * KB, 4 * KB, I8) for i in range(2)]
            onb = [at(64 * KB + i * 4 * KB, 4 * KB, U8) for i in range(2)]
            offb = [at(72 * KB + i * 4 * KB, 4 * KB, U8) for i in range(2)]
            adj_v = adj.rearrange("(g t p) j -> g p t j", t=IT1, p=P)
            H = NCH // 2
            acc = bank[0:4]

            with nc.Block() as block:
                @block.sync
                def _(sp):
                    with sp.Fori(0, NG1) as g:
                        for c in range(NCH):
                            wait_primed(sp, coded[c % 2], g * H + c // 2)
                            sp.dma_start(adjb[c % 2], adj_v[g, :, :, c * CHJ:(c + 1) * CHJ]).then_inc(adj_in[c % 2], 16)

                @block.scalar
                def _(act):
                    prime(act, *m_st, by=16)
                    with act.Fori(0, NG1) as g:
                        for c in range(NCH):
                            wait_primed(act, on_r[c % 2], g * H + c // 2)
                            sv = sbuf_[c % 2].rearrange("k (q i b) -> k q b i", q=QC, b=2)
                            for t in range(TC):
                                last = nc.scalar.activation(sv[:, t // 2, t % 2, :], urow[:, bass.ds(g * RG1, RG1)], ACT.Sign,
                                                            bias=negv[:, c * TC + t:c * TC + t + 1], scale=-1.0)
                            last.then_inc(sgn, 1)
                            for h in range(2):
                                wait_primed(act, out_of[2 * (c % 2) + h], g * H + c // 2 + 1)
                            act.dma_start(codes_d[g, c], mbuf[c % 4]).then_inc(m_st[c % 4], 16)
                    for i in range(4):
                        act.wait_ge(m_st[i], 16 * (1 + NG1 * NCH // 4))

                @block.vector
                def _(dve):
                    prime(dve, *coded, *on_r, *off_r, *out_of, acc_out)
                    def convert(g, c):
                        wait_apart(dve, adj_in[c % 2], (g * H + c // 2 + 1) * 16)
                        wait_primed(dve, tp_done[c % 2], (g * H + c // 2) * 2)
                        nc.vector.tensor_scalar(code[c % 2], adjb[c % 2].rearrange("p t j -> p (t j)"), 0.0, 1.5,
                                                ALU.max, ALU.min, saturate=False).then_inc(coded[c % 2], 1)

                    ws = Chain(dve, w_on)

                    def group(g, first=False, last=False):
                        for c in range(NCH):
                            if first:
                                split_on(ws, c)
                            wait_apart(dve, m_st[c % 4], (g * 2 + c // 4 + 1) * 16)
                            for h in range(2):
                                b = 2 * (c % 2) + h
                                wait_primed(dve, tp_done[c % 2], (g * H + c // 2) * 2 + h + 1)
                                nc.vector.tensor_copy(mbuf[c % 4].bitcast(U32)[:, 512 * h:512 * (h + 1)],
                                                      bank[4 + b][:, :].bitcast(U32)).then_inc(out_of[b], 1)
                            for h in range(2):
                                wait_primed(dve, out_of[2 * (c % 2) + h], g * H + c // 2 + 1)
                            wait_apart(dve, sgn, g * NCH + c + 1)
                            wait_primed(dve, used[c % 2], (g * H + c // 2) * IT1)
                            masks(dve, mbuf[c % 4].bitcast(U32), sbuf_[c % 2].bitcast(U32), onb[c % 2].bitcast(U32),
                                  offb[c % 2].bitcast(U32), on_r[c % 2], off_r[c % 2], g * H + c // 2)
                            if not (last and c + 2 >= NCH):
                                convert(g, c + 2)
                        wait_primed(dve, joined, g)
                        for it in range(IT1):
                            wait_primed(dve, used[1], (g * H + H - 1) * IT1 + it + 1)
                            nc.vector.tensor_reduce(rsum[:, it, :, :], acc[it][:, 0:2 * WC].rearrange(
                                "p (s j c) -> p s c j", s=2, j=3), AX.X, ALU.add).then_inc(acc_out, 1)

                    convert(0, 0)
                    convert(0, 1)
                    group(0, first=True)
                    with dve.Fori(1, NG1 - 1) as g:
                        group(g)
                    group(NG1 - 1, last=True)

                @block.gpsimd
                def _(pool):
                    prime(pool, joined)
                    ws = Chain(pool, w_off)
                    for c in range(NCH):
                        split_off(ws, c)
                    with pool.Fori(0, NG1) as g:
                        wait_primed(pool, acc_out, (g + 1) * IT1)
                        rows_join(pool, nc, g, IT1, acc_out, joined, pch)

                @block.tensor
                def _(pe):
                    prime(pe, *tp_done, *used)
                    def transposes(g, c):
                        wait_primed(pe, coded[c % 2], g * H + c // 2 + 1)
                        cv = code[c % 2].bitcast(BF16).rearrange("p (t q k) -> p t q k", t=IT1, q=QC)
                        for h in range(2):
                            b = 2 * (c % 2) + h
                            wait_primed(pe, out_of[b], g * H + c // 2)
                            tp = bank[4 + b][:, :].bitcast(BF16)
                            for q in range(2):
                                for t in range(IT1):
                                    last = nc.tensor.transpose(tp[:, q * 512 + t * P:q * 512 + (t + 1) * P],
                                                               cv[:, t, 2 * h + q, :], identb[:, :])
                            last.then_inc(tp_done[c % 2], 1)

                    def group(g, last):
                        for c in range(NCH):
                            if not (last and c + 1 >= NCH):
                                transposes(g, c + 1)
                            pe.wait_ge(w_on, SPLIT * (c + 1))
                            pe.wait_ge(w_off, SPLIT * (c + 1))
                            wait_primed(pe, off_r[c % 2], g * H + c // 2 + 1)
                            if c == 0:
                                wait_primed(pe, acc_out, g * IT1)
                            for it in range(IT1):
                                if c == 0:
                                    nc.tensor.matmul(acc[it][:, 0:2 * WC], identb[:, :], zeros[:, 0:2 * WC], start=True, stop=False,
                                                     skip_group_check=True)
                                on_c, off_c = columns(onb[c % 2], 1, it), columns(offb[c % 2], 1, it)
                                for t in range(TC):
                                    nc.tensor.matmul(acc[it][:, 0:WC], on_c[t], wsplit[:, c * TC + t, 0:WC], start=False,
                                                     stop=False, skip_group_check=True)
                                    end = nc.tensor.matmul(acc[it][:, WC:2 * WC], off_c[t], wsplit[:, c * TC + t, WC:2 * WC], start=False,
                                                           stop=(c == NCH - 1 and t == TC - 1), skip_group_check=True)
                                end.then_inc(used[c % 2], 1)

                    transposes(0, 0)
                    with pe.Fori(0, NG1 - 1) as g:
                        group(g, False)
                    group(NG1 - 1, True)

        def later_layer():
            s = lambda n: sem(f"s_{n}")
            two = lambda n: [sem(f"s_{n}{i}") for i in range(2)]
            m_in, on_r, off_r, used = two("codes_loaded"), two("on_ready"), two("off_ready"), two("masks_used")
            sgn, joined, pch = s("signs"), s("rows_joined"), s("pool_chain")
            w_on, w_off = s("on_side_split"), s("off_side_split")
            acc_out = [s(f"sums_taken{i}") for i in range(IT2)]
            mbuf, sbuf_, onb, offb = ([at((8 * i + 16 * k) * KB, 8 * KB, dt) for i in range(2)]
                                      for k, dt in enumerate((U8, I8, U8, U8)))
            H = NCH // 2
            GH = IT2 // IT1
            with nc.Block() as block:
                @block.sync
                def _(sp):
                    with sp.Fori(0, NG2) as g:
                        for c in range(NCH):
                            wait_primed(sp, off_r[c % 2], g * H + c // 2)
                            sp.dma_start(mbuf[c % 2].rearrange("p (a x) -> p a x", a=GH),
                                         codes_d[bass.ds(g * GH, GH), c].rearrange("a p x -> p a x")).then_inc(m_in[c % 2], 16)

                @block.scalar
                def _(act):
                    with act.Fori(0, NG2) as g:
                        for c in range(NCH):
                            wait_primed(act, on_r[c % 2], g * H + c // 2)
                            sv = sbuf_[c % 2].rearrange("k (a q i b) -> k q b a i", a=GH, q=QC, b=2)
                            for t in range(TC):
                                last = nc.scalar.activation(sv[:, t // 2, t % 2, :, :],
                                                            urow[:, bass.ds(g * RG2, RG2)].rearrange("p (a i) -> p a i", a=GH),
                                                            ACT.Sign, bias=negv[:, c * TC + t:c * TC + t + 1], scale=-1.0)
                            last.then_inc(sgn, 1)

                @block.vector
                def _(dve):
                    prime(dve, *on_r, *off_r, *acc_out)
                    ws = Chain(dve, w_on)

                    def chunk(g, c):
                        n = g * H + c // 2
                        wait_apart(dve, m_in[c % 2], (n + 1) * 16)
                        wait_apart(dve, sgn, g * NCH + c + 1)
                        wait_primed(dve, used[c % 2], n * IT2)
                        masks(dve, mbuf[c % 2].bitcast(U32), sbuf_[c % 2].bitcast(U32), onb[c % 2].bitcast(U32),
                              offb[c % 2].bitcast(U32), on_r[c % 2], off_r[c % 2], n)

                    def group(g, first=False, last=False):
                        for c in range(1, NCH):
                            if first:
                                split_on(ws, c)
                            chunk(g, c)
                        if not last:
                            chunk(g, NCH)
                        wait_primed(dve, joined, g)
                        for it in range(IT2):
                            wait_primed(dve, used[1], (g * H + H - 1) * IT2 + it + 1)
                            nc.vector.tensor_reduce(rsum[:, it, :, :], bank[it][:, 0:2 * WC].rearrange(
                                "p (s j c) -> p s c j", s=2, j=3), AX.X, ALU.add).then_inc(acc_out[it], 1)

                    split_on(ws, 0)
                    chunk(0, 0)
                    group(0, first=True)
                    with dve.Fori(1, NG2 - 1) as g:
                        group(g)
                    group(NG2 - 1, last=True)

                @block.gpsimd
                def _(pool):
                    prime(pool, joined)
                    ws = Chain(pool, w_off)
                    for c in range(NCH):
                        split_off(ws, c)
                    with pool.Fori(0, NG2) as g:
                        for it in range(IT2):
                            wait_primed(pool, acc_out[it], g + 1)
                        rows_join(pool, nc, g, IT2, None, joined, pch)

                @block.tensor
                def _(pe):
                    prime(pe, *used)
                    with pe.Fori(0, NG2) as g:
                        for c in range(NCH):
                            pe.wait_ge(w_on, SPLIT * (c + 1))
                            pe.wait_ge(w_off, SPLIT * (c + 1))
                            wait_primed(pe, off_r[c % 2], g * H + c // 2 + 1)
                            for it in range(IT2):
                                if c == 0:
                                    wait_primed(pe, acc_out[it], g)
                                    nc.tensor.matmul(bank[it][:, 0:2 * WC], identb[:, :], zeros[:, 0:2 * WC], start=True, stop=False,
                                                     skip_group_check=True)
                                on_c, off_c = columns(onb[c % 2], GH, it), columns(offb[c % 2], GH, it)
                                for t in range(TC):
                                    nc.tensor.matmul(bank[it][:, 0:WC], on_c[t], wsplit[:, c * TC + t, 0:WC], start=False,
                                                     stop=False, skip_group_check=True)
                                    end = nc.tensor.matmul(bank[it][:, WC:2 * WC], off_c[t], wsplit[:, c * TC + t, WC:2 * WC], start=False,
                                                           stop=(c == NCH - 1 and t == TC - 1), skip_group_check=True)
                                end.then_inc(used[c % 2], 1)

        def mean_layer():
            s = lambda n: sem(f"m_{n}")
            S4 = 4
            four = lambda n: [sem(f"m_{n}{i}") for i in range(S4)]
            m_in, mixed, eq, used = four("codes_loaded"), four("mixed"), four("equal_one"), four("masks_used")
            biased = s("bias_added")
            taken = [s(f"sums_taken{i}") for i in range(3)]
            rd, vch = s("degree_inverted"), s("vchain")
            spare = wsplit[:, :, :].rearrange("p t c -> p (t c)")[:, T * (2 * C + 1):].bitcast(U8)
            mbuf = [spare[:, 8 * i * KB:8 * (i + 1) * KB] for i in range(S4)]
            ebuf = [at(8 * i * KB, 8 * KB, U8) for i in range(S4)]
            H = NCH // S4
            GH = IT2 // IT1
            MC = 2 * C + 1
            with nc.Block() as block:
                @block.sync
                def _(sp):
                    with sp.Fori(0, NG2) as g:
                        for c in range(NCH):
                            wait_primed(sp, mixed[c % S4], g * H + c // S4)
                            sp.dma_start(mbuf[c % S4].rearrange("p (a x) -> p a x", a=GH),
                                         codes_d[bass.ds(g * GH, GH), c].rearrange("a p x -> p a x")).then_inc(m_in[c % S4], 16)

                @block.vector
                def _(dve):
                    prime(dve, *mixed, *taken)
                    with dve.Fori(0, NG2) as g:
                        for c in range(NCH):
                            n = g * H + c // S4
                            wait_apart(dve, m_in[c % S4], (n + 1) * 16)
                            wait_primed(dve, used[c % S4], n * IT2)
                            m32, e32 = mbuf[c % S4].bitcast(U32), ebuf[c % S4].bitcast(U32)
                            nc.vector.scalar_tensor_tensor(e32, m32, 1, m32, ALU.logical_shift_left,
                                                           ALU.bitwise_xor).then_inc(mixed[c % S4], 1)
                            wait_primed(dve, mixed[c % S4], n + 1)
                            nc.vector.tensor_scalar(e32, e32, 0x08080808, None, ALU.bitwise_and).then_inc(eq[c % S4], 1)
                        for k in range(3):
                            nt = min(3, IT2 - 3 * k)
                            wait_primed(dve, used[S4 - 1], (g * H + H - 1) * IT2 + 3 * k + nt)
                            av = bank[k][:, 0:nt * MC].rearrange("p (t c) -> p t c", c=MC)
                            dst = nx[:, bass.ds(g * IT2 + 3 * k, nt), 0:C]
                            ch = Chain(dve, vch, g * 3 + k)
                            nc.vector.reciprocal(nonb[:, 0:nt], av[:, :, 2 * C])
                            ch.step(nc.vector.tensor_reduce(pa[:, 0:nt, 0:C], av[:, :, 0:2 * C].rearrange(
                                "p t (j c) -> p t c j", j=2), AX.X, ALU.add))
                            nc.vector.scalar_tensor_tensor(dst, pa[:, 0:nt, 0:C], 1.0 / FSC,
                                                           nonb[:, 0:nt].unsqueeze(2).to_broadcast([P, nt, C]),
                                                           ALU.mult, ALU.mult).then_inc(taken[k], 1)
                            wait_primed(dve, taken[k], g + 1)

                @block.gpsimd
                def _(pool):
                    nc.gpsimd.tensor_tensor(xr, xr, b1b[:, :].unsqueeze(1).to_broadcast([P, T, C]), ALU.add).then_inc(biased, 1)

                @block.tensor
                def _(pe):
                    prime(pe, *used)
                    with pe.Fori(0, NG2) as g:
                        for c in range(NCH):
                            wait_apart(pe, eq[c % S4], g * H + c // S4 + 1)
                            for it in range(IT2):
                                k, o = it // 3, (it % 3) * MC
                                if c == 0 and it % 3 == 0:
                                    wait_primed(pe, taken[k], g)
                                    nc.tensor.matmul(bank[k][:, 0:3 * MC], identb[:, :], zeros[:, 0:3 * MC], start=True, stop=False,
                                                     skip_group_check=True)
                                cols = columns(ebuf[c % S4], GH, it)
                                for t in range(TC):
                                    end = nc.tensor.matmul(bank[k][:, o:o + MC], cols[t], wf16[:, c * TC + t, :], start=False,
                                                           stop=(c == NCH - 1 and t == TC - 1), skip_group_check=True)
                                end.then_inc(used[c % S4], 1)

        def finish():
            s = lambda n: sem(f"o_{n}")
            tp, cp, pr, ad, st = s("transposed"), s("copied"), s("products"), s("added"), s("stored")
            NB = 16
            nt = [at(i * 2 * KB, 2 * KB, FP32) for i in range(2)]
            with nc.Block() as block:
                @block.tensor
                def _(pe):
                    def transposes(k):
                        if k >= 2:
                            pe.wait_ge(cp, k - 1)
                        for i in range(4):
                            last = nc.tensor.transpose(bank[k % 2][:, i * P:(i + 1) * P], nx[:, 4 * k + i, :], identf[:, :])
                        last.then_inc(tp, 1)
                    transposes(0)
                    for k in range(NB):
                        if k + 1 < NB:
                            transposes(k + 1)
                        pe.wait_ge(cp, k + 1)
                        if k >= 2:
                            pe.wait_ge(ad, k - 1)
                        for i in range(4):
                            last = nc.tensor.matmul(bank[2 + k % 2][:, i * C:(i + 1) * C], nt[k % 2][:, i * P:(i + 1) * P], w1s[:, :],
                                                    start=True, stop=True)
                        last.then_inc(pr, 1)

                @block.scalar
                def _(act):
                    for k in range(NB):
                        act.wait_ge(tp, k + 1)
                        if k >= 2:
                            act.wait_ge(pr, k - 1)
                        nc.scalar.activation(nt[k % 2], bank[k % 2][:, :], ACT.Copy).then_inc(cp, 1)

                @block.vector
                def _(dve):
                    for k in range(NB):
                        dve.wait_ge(pr, k + 1)
                        nc.vector.tensor_tensor(xr[:, 4 * k:4 * k + 4, :], xr[:, 4 * k:4 * k + 4, :],
                                                bank[2 + k % 2][:, 0:4 * C].rearrange("p (t c) -> p t c", c=C),
                                                ALU.add).then_inc(ad, 1)

                @block.sync
                def _(sp):
                    for k in range(4):
                        sp.wait_ge(ad, 4 * k + 4)
                        sp.dma_start(out_v[:, 8 * k:8 * k + 8, :], pairs(xr)[:, 8 * k:8 * k + 8, :]).then_inc(st, 16)
                    sp.wait_ge(st, 64)

        boundary(0)
        first_layer()
        boundary(1)
        later_layer()
        boundary(2)
        mean_layer()
        finish()


_INS = ["x", "adj", "L0_gnn_W", "L0_gnn_lin_w", "L0_gnn_lin_b", "L0_gnn_attn", "L0_gnn_mlp_w", "L0_gnn_mlp_b",
        "L1_gnn_weight", "L1_gnn_bias"]


def kernel(**inputs):
    import numpy as _np
    import concourse.bacc as _bacc
    from concourse import mybir as _mybir
    from concourse.bass_utils import run_bass_kernel_spmd as _run

    nc = _bacc.Bacc("TRN2", target_bir_lowering=False, num_devices=1)
    arrays, args = {}, []
    for name in _INS:
        a = _np.ascontiguousarray(inputs[name])
        arrays[f"in_{name}"] = a
        args.append(nc.dram_tensor(f"in_{name}", a.shape, _mybir.dt.from_np(a.dtype), kind="ExternalInput").ap())
    o = nc.dram_tensor("out_0", (N, C), FP32, kind="ExternalOutput").ap()
    gnn_program(nc, *args, o)
    r = _run(nc, [arrays], core_ids=[0])
    return r.results[0]["out_0"]
```
